# Optimizing a Trainium2 kernel written in Bass

```python
import numpy as np
import jax
import jax.numpy as jnp

def _softmax(x, axis=-1):
    return jax.nn.softmax(x, axis=axis)

def _gelu(x):
    return jax.nn.gelu(x, approximate=True)

def _silu(x):
    return jax.nn.silu(x)

def _sigmoid(x):
    return jax.nn.sigmoid(x)

def _layernorm(x, axis=-1, eps=1e-05):
    m = jnp.mean(x, axis=axis, keepdims=True)
    v = jnp.var(x, axis=axis, keepdims=True)
    return (x - m) / jnp.sqrt(v + eps)

def _scatter_add(tgt, idx, src, axis=0):
    return tgt.at[idx].add(src)

def _segment_sum(src, seg, n):
    return jax.ops.segment_sum(src, seg, n)
kernel_name = 'mk_macaron_d1_jaxref_r4_09c233'

def setup_inputs(seed: int=0):
    np.random.seed(seed)
    _w = jnp.asarray

    def _L0_attn_setup():
        import jax, jax.numpy as jnp
        import numpy as np
        B, T, H, NH = (2, 512, 256, 16)
        D = H // NH
        K_CONV = 4

        def _dwconv_silu(x, w):
            Kc = w.shape[1]
            xp = jnp.pad(x, ((0, 0), (Kc - 1, 0), (0, 0))).transpose(0, 2, 1)
            y = jax.lax.conv_general_dilated(xp, w[:, None, :], (1,), 'VALID', feature_group_count=w.shape[0], dimension_numbers=('NCH', 'OIH', 'NCH'))
            return jax.nn.silu(y.transpose(0, 2, 1))

        def _l2norm(x, eps=1e-06):
            return x * jax.lax.rsqrt(jnp.sum(x * x, -1, keepdims=True) + eps)

        def _forward(hidden, Wq, Wk, Wv, conv_q, conv_k, conv_v, Wb, Wa, A_log, dt_bias, Wg, norm_w, Wo):
            Bh, Tt, Hh = hidden.shape
            nh = A_log.shape[0]
            d = Hh // nh
            q = _dwconv_silu(hidden @ Wq.T, conv_q).reshape(Bh, Tt, nh, d)
            k = _dwconv_silu(hidden @ Wk.T, conv_k).reshape(Bh, Tt, nh, d)
            v = _dwconv_silu(hidden @ Wv.T, conv_v).reshape(Bh, Tt, nh, d)
            q = _l2norm(q) * d ** (-0.5)
            k = _l2norm(k)
            beta = jax.nn.sigmoid(hidden @ Wb.T)
            g = -jnp.exp(A_log) * jax.nn.softplus(hidden @ Wa.T + dt_bias)

            def step(S, inp):
                qt, kt, vt, gt, bt = inp
                S = S * jnp.exp(gt)[..., None, None]
                pred = jnp.einsum('bhk,bhkv->bhv', kt, S)
                dv = (vt - pred) * bt[..., None]
                S = S + jnp.einsum('bhk,bhv->bhkv', kt, dv)
                ot = jnp.einsum('bhk,bhkv->bhv', qt, S)
                return (S, ot)
            xs = (q.transpose(1, 0, 2, 3), k.transpose(1, 0, 2, 3), v.transpose(1, 0, 2, 3), g.transpose(1, 0, 2), beta.transpose(1, 0, 2))
            S0 = jnp.zeros((Bh, nh, d, d), hidden.dtype)
            _, o = jax.lax.scan(step, S0, xs)
            o = o.transpose(1, 0, 2, 3)
            gate = (hidden @ Wg.T).reshape(Bh, Tt, nh, d)
            o = o * jax.lax.rsqrt(jnp.mean(o * o, -1, keepdims=True) + 1e-05) * norm_w
            o = o * jax.nn.silu(gate)
            return o.reshape(Bh, Tt, Hh) @ Wo.T
        key = jax.random.key(seed)
        ks = jax.random.split(key, 16)
        s = 0.02
        return {'hidden': jax.random.normal(ks[0], (B, T, H), jnp.float32), 'Wq': jax.random.normal(ks[1], (H, H), jnp.float32) * s, 'Wk': jax.random.normal(ks[2], (H, H), jnp.float32) * s, 'Wv': jax.random.normal(ks[3], (H, H), jnp.float32) * s, 'conv_q': jax.random.normal(ks[4], (H, K_CONV), jnp.float32) * 0.5, 'conv_k': jax.random.normal(ks[5], (H, K_CONV), jnp.float32) * 0.5, 'conv_v': jax.random.normal(ks[6], (H, K_CONV), jnp.float32) * 0.5, 'Wb': jax.random.normal(ks[7], (NH, H), jnp.float32) * s, 'Wa': jax.random.normal(ks[8], (NH, H), jnp.float32) * s, 'A_log': jnp.log(jax.random.uniform(ks[9], (NH,), jnp.float32, 1.0, 16.0)), 'dt_bias': jnp.log(jnp.expm1(jax.random.uniform(ks[10], (NH,), jnp.float32, 0.001, 0.1))), 'Wg': jax.random.normal(ks[11], (H, H), jnp.float32) * s, 'norm_w': jnp.ones((D,), jnp.float32), 'Wo': jax.random.normal(ks[12], (H, H), jnp.float32) * s}
    _L0_attn_in = _L0_attn_setup()

    def _L0_ffn_setup():
        import jax, jax.numpy as jnp
        import numpy as np
        DIM = 256

        def _reference_tuple_inner(x, W_r, W_k, W_v, mu_r, mu_k):
            B, T, C = x.shape
            x_prev = jnp.concatenate([jnp.zeros((B, 1, C), x.dtype), x[:, :-1, :]], axis=1)
            xr = mu_r * x + (1.0 - mu_r) * x_prev
            xk = mu_k * x + (1.0 - mu_k) * x_prev
            r = jax.nn.sigmoid(jnp.einsum('btc,dc->btd', xr, W_r))
            k = jnp.einsum('btc,dc->btd', xk, W_k)
            k_act = jnp.square(jax.nn.relu(k))
            out = r * jnp.einsum('btc,dc->btd', k_act, W_v)
            new_state = x[:, -1, :]
            return (out, new_state)
        key = jax.random.key(seed)
        ks = jax.random.split(key, 6)
        B, T, C = (8, 512, DIM)
        x = jax.random.normal(ks[0], (B, T, C), dtype=jnp.float32)
        s = 1.0 / np.sqrt(C)
        W_r = jax.random.uniform(ks[1], (C, C), jnp.float32, -s, s)
        W_k = jax.random.uniform(ks[2], (C, C), jnp.float32, -s, s)
        W_v = jax.random.uniform(ks[3], (C, C), jnp.float32, -s, s)
        mu_r = jax.random.uniform(ks[4], (C,), jnp.float32)
        mu_k = jax.random.uniform(ks[5], (C,), jnp.float32)
        return {'x': x, 'W_r': W_r, 'W_k': W_k, 'W_v': W_v, 'mu_r': mu_r, 'mu_k': mu_k}
    _L0_ffn_in = _L0_ffn_setup()
    _d = {'L0_attn_hidden': _L0_attn_in['hidden'], 'L0_attn_Wq': _L0_attn_in['Wq'], 'L0_attn_Wk': _L0_attn_in['Wk'], 'L0_attn_Wv': _L0_attn_in['Wv'], 'L0_attn_conv_q': _L0_attn_in['conv_q'], 'L0_attn_conv_k': _L0_attn_in['conv_k'], 'L0_attn_conv_v': _L0_attn_in['conv_v'], 'L0_attn_Wb': _L0_attn_in['Wb'], 'L0_attn_Wa': _L0_attn_in['Wa'], 'L0_attn_A_log': _L0_attn_in['A_log'], 'L0_attn_dt_bias': _L0_attn_in['dt_bias'], 'L0_attn_Wg': _L0_attn_in['Wg'], 'L0_attn_norm_w': _L0_attn_in['norm_w'], 'L0_attn_Wo': _L0_attn_in['Wo'], 'L0_ffn_W_r': _L0_ffn_in['W_r'], 'L0_ffn_W_k': _L0_ffn_in['W_k'], 'L0_ffn_W_v': _L0_ffn_in['W_v'], 'L0_ffn_mu_r': _L0_ffn_in['mu_r'], 'L0_ffn_mu_k': _L0_ffn_in['mu_k']}
    _x0 = _d['L0_attn_hidden']
    _d['L0_attn_hidden'] = jax.random.normal(jax.random.fold_in(jax.random.key(seed), 1), (2, 4096, 256), dtype=_x0.dtype)
    del _x0
    return _d

def reference(L0_attn_hidden, L0_attn_Wq, L0_attn_Wk, L0_attn_Wv, L0_attn_conv_q, L0_attn_conv_k, L0_attn_conv_v, L0_attn_Wb, L0_attn_Wa, L0_attn_A_log, L0_attn_dt_bias, L0_attn_Wg, L0_attn_norm_w, L0_attn_Wo, L0_ffn_W_r, L0_ffn_W_k, L0_ffn_W_v, L0_ffn_mu_r, L0_ffn_mu_k):

    def _L0_attn_ref(hidden, Wq, Wk, Wv, conv_q, conv_k, conv_v, Wb, Wa, A_log, dt_bias, Wg, norm_w, Wo):
        import jax, jax.numpy as jnp
        import numpy as np
        B, T, H, NH = (2, 512, 256, 16)
        D = H // NH
        K_CONV = 4

        def _dwconv_silu(x, w):
            Kc = w.shape[1]
            xp = jnp.pad(x, ((0, 0), (Kc - 1, 0), (0, 0))).transpose(0, 2, 1)
            y = jax.lax.conv_general_dilated(xp, w[:, None, :], (1,), 'VALID', feature_group_count=w.shape[0], dimension_numbers=('NCH', 'OIH', 'NCH'))
            return jax.nn.silu(y.transpose(0, 2, 1))

        def _l2norm(x, eps=1e-06):
            return x * jax.lax.rsqrt(jnp.sum(x * x, -1, keepdims=True) + eps)

        def _forward(hidden, Wq, Wk, Wv, conv_q, conv_k, conv_v, Wb, Wa, A_log, dt_bias, Wg, norm_w, Wo):
            Bh, Tt, Hh = hidden.shape
            nh = A_log.shape[0]
            d = Hh // nh
            q = _dwconv_silu(hidden @ Wq.T, conv_q).reshape(Bh, Tt, nh, d)
            k = _dwconv_silu(hidden @ Wk.T, conv_k).reshape(Bh, Tt, nh, d)
            v = _dwconv_silu(hidden @ Wv.T, conv_v).reshape(Bh, Tt, nh, d)
            q = _l2norm(q) * d ** (-0.5)
            k = _l2norm(k)
            beta = jax.nn.sigmoid(hidden @ Wb.T)
            g = -jnp.exp(A_log) * jax.nn.softplus(hidden @ Wa.T + dt_bias)

            def step(S, inp):
                qt, kt, vt, gt, bt = inp
                S = S * jnp.exp(gt)[..., None, None]
                pred = jnp.einsum('bhk,bhkv->bhv', kt, S)
                dv = (vt - pred) * bt[..., None]
                S = S + jnp.einsum('bhk,bhv->bhkv', kt, dv)
                ot = jnp.einsum('bhk,bhkv->bhv', qt, S)
                return (S, ot)
            xs = (q.transpose(1, 0, 2, 3), k.transpose(1, 0, 2, 3), v.transpose(1, 0, 2, 3), g.transpose(1, 0, 2), beta.transpose(1, 0, 2))
            S0 = jnp.zeros((Bh, nh, d, d), hidden.dtype)
            _, o = jax.lax.scan(step, S0, xs)
            o = o.transpose(1, 0, 2, 3)
            gate = (hidden @ Wg.T).reshape(Bh, Tt, nh, d)
            o = o * jax.lax.rsqrt(jnp.mean(o * o, -1, keepdims=True) + 1e-05) * norm_w
            o = o * jax.nn.silu(gate)
            return o.reshape(Bh, Tt, Hh) @ Wo.T
        return _forward(hidden, Wq, Wk, Wv, conv_q, conv_k, conv_v, Wb, Wa, A_log, dt_bias, Wg, norm_w, Wo)

    def _L0_ffn_ref(x, W_r, W_k, W_v, mu_r, mu_k):
        import jax, jax.numpy as jnp
        import numpy as np
        DIM = 256

        def _reference_tuple_inner(x, W_r, W_k, W_v, mu_r, mu_k):
            B, T, C = x.shape
            x_prev = jnp.concatenate([jnp.zeros((B, 1, C), x.dtype), x[:, :-1, :]], axis=1)
            xr = mu_r * x + (1.0 - mu_r) * x_prev
            xk = mu_k * x + (1.0 - mu_k) * x_prev
            r = jax.nn.sigmoid(jnp.einsum('btc,dc->btd', xr, W_r))
            k = jnp.einsum('btc,dc->btd', xk, W_k)
            k_act = jnp.square(jax.nn.relu(k))
            out = r * jnp.einsum('btc,dc->btd', k_act, W_v)
            new_state = x[:, -1, :]
            return (out, new_state)
        return _reference_tuple_inner(x, W_r, W_k, W_v, mu_r, mu_k)[0]
    x = L0_attn_hidden
    x = x + 0.5 * _L0_ffn_ref(_layernorm(x, axis=-1), L0_ffn_W_r, L0_ffn_W_k, L0_ffn_W_v, L0_ffn_mu_r, L0_ffn_mu_k)
    x = x + _L0_attn_ref(_layernorm(x, axis=-1), L0_attn_Wq, L0_attn_Wk, L0_attn_Wv, L0_attn_conv_q, L0_attn_conv_k, L0_attn_conv_v, L0_attn_Wb, L0_attn_Wa, L0_attn_A_log, L0_attn_dt_bias, L0_attn_Wg, L0_attn_norm_w, L0_attn_Wo)
    x = x + 0.5 * _L0_ffn_ref(_layernorm(x, axis=-1), L0_ffn_W_r, L0_ffn_W_k, L0_ffn_W_v, L0_ffn_mu_r, L0_ffn_mu_k)
    return x

_drawn_inputs = setup_inputs


def setup_inputs(seed=0):
    import zlib

    import numpy as np

    out = dict(_drawn_inputs(seed))
    spreads = {'L0_attn_norm_w': (1.0, 0.6)}
    factors = {'L0_attn_Wb': 8.0,
     'L0_attn_Wa': 8.0,
     'L0_attn_A_log': 3.884,
     'L0_attn_dt_bias': 3.963,
     'L0_ffn_W_r': 3.17,
     'L0_ffn_mu_r': 6.38}
    for name, (base, spread) in spreads.items():
        noise = np.random.default_rng([zlib.crc32(name.encode()), seed]).standard_normal(out[name].shape)
        drawn = base * np.exp(spread * noise) if base else spread * noise
        out[name] = jnp.asarray(drawn.astype(out[name].dtype))
    for name, factor in factors.items():
        out[name] = (out[name] * factor).astype(out[name].dtype)
    return out
```

```python
from contextlib import ExitStack

import numpy as np

import concourse.bass as bass
from concourse import mybir

F32 = mybir.dt.float32
BF16 = mybir.dt.bfloat16
ACT = mybir.ActivationFunctionType
ALU = mybir.AluOpType
AX_X = mybir.AxisListType.X

B, SEQ, H, NH = 2, 4096, 256, 16
D = H // NH
C = 16
KC = 4
P = 128
TG = 256
GROUPS = SEQ // TG
M = H // P
NT = B * TG // P
COLS = M * B * TG
PACKS = COLS // C
NCH = TG // C
HP = P // C
HALF = B * TG
BANK = 512


def macaron_kernel(nc, x, wts, ffn_mu, convw, wab, hp, consts, out):
    with ExitStack() as ctx:
        def sb(name, shape, dt=F32):
            return ctx.enter_context(nc.sbuf_tensor(name, shape, dt))

        def sem(name):
            return ctx.enter_context(nc.semaphore(name))

        w = {n: sb(f"w_{n}", [P, M, H]) for n in wts}
        w_ab = sb("w_ab", [P, M, 2 * NH])
        mu = sb("mu", [P, 2, M])
        cw = sb("cw", [P, 3, M, KC])
        TH = NT * NH
        headp = sb("headp", [P, 1 + 2 * TH])
        normw, a_log, dt_b = headp[:, 0:1], headp[:, 1:1 + TH], headp[:, 1 + TH:]
        neg_a = sb("neg_a", [P, TH])
        cst = sb("cst", [P, 2, P])
        msk = sb("msk", [P, 3, C])
        notfirst = sb("notfirst", [P, COLS])
        ident, same_head = cst[:, 0, :], cst[:, 1, :]

        X = sb("X", [P, NT, H])
        XN = sb("XN", [P, COLS])
        XT = sb("XT", [P, M, B, 1 + TG])
        XTc = sb("XTc", [P, 2, M, B, 1])
        DX = sb("DX", [P, COLS])
        XR = sb("XR", [P, COLS])
        XK = sb("XK", [P, COLS])
        KA = sb("KA", [P, COLS])
        R = sb("R", [P, COLS])
        YT = sb("YT", [P, COLS])
        GS = sb("GS", [P, COLS])
        VS = sb("VS", [P, COLS])
        KQI = sb("KQI", [P, 3, COLS])
        E = sb("E", [P, COLS])
        EE = sb("EE", [P, COLS])
        arena = sb("arena", [P, 2 * C * P + 8 * 8 * HP])
        CT = KC - 1
        CIN = [arena[:, i * (M * B * (CT + TG)):(i + 1) * (M * B * (CT + TG))]
               .rearrange("p (m b t) -> p m b t", m=M, b=B) for i in range(3)]
        Au = arena[0:PACKS, 0:C * P]
        Tu = arena[0:PACKS, C * P:2 * C * P]
        prod = arena[0:PACKS, 2 * C * P:]
        OT = arena[:, 0:COLS]
        cinc = sb("cinc", [P, 3, M, B, CT])
        S_in = sb("S_in", [P, M * B, D])
        spread_a = sb("spread_a", [P, HP, COLS])
        spread_b = sb("spread_b", [P, HP, COLS])
        spread_c = sb("spread_c", [P, HP, COLS])
        st = sb("st", [P, NT, 6])
        mv = sb("mv", [P, NT, 2])
        sd = sb("sd", [P, NT, 1])
        rstd = sb("rstd", [P, NT, 1])
        sp = sb("sp", [P, 7, TH])
        be = sb("be", [P, PACKS])
        fd = sb("fd", [P, PACKS])
        fD = sb("fD", [P, B, M, D])
        ps = ctx.enter_context(nc.psum_tensor("ps", [P, 8 * BANK], F32))

        def bank(i, n=1):
            return ps[:, i * BANK:(i + n) * BANK]

        names = ("weights_in x_in out_stored zeroed setup_vec setup_act "
                 "stats_ready std_ready xn_ready xT_psum xT_ready mixed k_psum k_relu k_squared r_psum r_ready v_psum "
                 "x1_ready proj_psum gate_ready conv_in qkv_conv qkv_silu sq_ready ss_psum ss_ready ss_root qk_ready "
                 "ab_psum z_ready e1_ready u_ready ln_ready beta_ready g_ready rep_psum rep_ready csum_ready ee_ready "
                 "dsum_ready e_ready vb_ready masks_ready kspread vspread gram_psum gram_out a_psum a_ready inv_ready t_psum tt_ready "
                 "ttb_ready tspread ktspread uw_psum uw_ready wspread sspread dspread s0_ready pred_psum delta_ready snew_psum s_ready "
                 "o_psum osq_ready oss_psum oss_ready oss_root og_ready wo_psum x2_ready act_step vec_step pool_step").split()
        s = {n: sem(n) for n in names}

        def bc(ap2, n):
            return bass.AP(tensor=ap2.tensor, offset=ap2.offset, ap=[list(ap2.ap[0]), [0, n], list(ap2.ap[1])])

        def rep(ap2, n):
            return bass.AP(tensor=ap2.tensor, offset=ap2.offset, ap=[list(ap2.ap[0]), list(ap2.ap[1]), [0, n]])

        def packs(ap2):
            return ap2.rearrange("p (k c) -> p k c", c=C)

        def turned(ap2):
            return ap2.rearrange("p (c k) -> p k c", c=C)

        def block_of(spread, i):
            return spread[:].rearrange("p h (c k) -> p (h c) k", c=C)[:, :, i]

        x_v = x.rearrange("b (g q p) c -> g p b q c", p=P, q=TG // P)
        o_v = out.rearrange("b (g q p) c -> g p b q c", p=P, q=TG // P)

        VEC_STEPS, ACT_STEPS = VEC_N, ACT_N

        class Steps:
            def __init__(self, eng, semaphore, per_group):
                self.eng, self.sem, self.per, self.k, self.g = eng, semaphore, per_group, 0, 0

            def done(self, ins):
                ins.then_inc(self.sem, 1)
                self.k += 1

            def settle(self):
                self.eng.wait_ge(self.sem, self.g * self.per + self.k)

        block = ctx.enter_context(nc.Block())

        @block.sync
        def _(sp_):
            n_in = 0
            for n, ap in wts.items():
                sp_.dma_start(w[n][:], ap.rearrange("(k p) d -> p k d", p=P)).then_inc(s["weights_in"], 16)
                n_in += 1
            for dst, src in ((w_ab[:], wab.rearrange("(k p) d -> p k d", p=P)), (mu[:], ffn_mu), (cw[:], convw),
                             (headp[:], hp),
                             (cst[:], consts[:, 0:2 * P].rearrange("p (a b) -> p a b", a=2)),
                             (msk[:], consts[:, 2 * P:2 * P + 3 * C].rearrange("p (a b) -> p a b", a=3)),
                             (notfirst[:], consts[:, 2 * P + 3 * C:2 * P + 3 * C + COLS]),
                             (KQI[:, 2, :], consts[:, 2 * P + 3 * C + COLS:2 * P + 3 * C + 2 * COLS])):
                sp_.dma_start(dst, src).then_inc(s["weights_in"], 16)
                n_in += 1
            assert n_in == N_IN

            def spread(dst, src, signal):
                for h in range(HP):
                    sp_.dma_start(dst[C * h:C * h + C, h, :], src[C * h:C * h + C, :]).then_inc(signal, 16)

            sp_.wait_ge(s["zeroed"], N_ZERO)
            with sp_.Fori(0, GROUPS) as g:
                sp_.wait_ge(s["qk_ready"], g * 2 + 2)
                spread(spread_a, KQI[:, 0, :], s["kspread"])
                sp_.wait_ge(s["vb_ready"], g + 1)
                spread(spread_b, YT, s["vspread"])
                sp_.wait_ge(s["gram_out"], g * 4 + 4)
                spread(spread_b, XN, s["ktspread"])
                sp_.wait_ge(s["tt_ready"], g + 1)
                spread(spread_a, VS, s["tspread"])
                sp_.wait_ge(s["uw_ready"], g * 2 + 2)
                spread(spread_c, E, s["wspread"])
                sp_.wait_ge(s["s_ready"], (g + 1) * NCH * B)
                spread(spread_a, KA, s["sspread"])
                spread(spread_b, XR, s["dspread"])

        @block.tensor
        def _(pe):
            mm = nc.tensor.matmul

            def turn(u, g):
                pe.wait_ge(s["xn_ready"], g * 3 + u + 1)
                for k in range(M):
                    for j in range(NT):
                        last = nc.tensor.transpose(ps[:, k * HALF + j * P:k * HALF + (j + 1) * P],
                                                   XN[:, j * H + k * P:j * H + (k + 1) * P], ident)
                last.then_inc(s["xT_psum"], 1)

            def cols_out(dst, wt, src, signal):
                for m in range(M):
                    for k in range(M):
                        last = mm(bank(dst + m), wt[:, k, m * P:(m + 1) * P], src[:, k * HALF:(k + 1) * HALF],
                                  start=(k == 0), stop=(k == M - 1))
                last.then_inc(signal, 1)

            def rows_out(dst, wt, src, signal):
                for j in range(NT):
                    for k in range(M):
                        last = mm(ps[:, dst * BANK + j * H:dst * BANK + (j + 1) * H],
                                  src[:, k * HALF + j * P:k * HALF + (j + 1) * P], wt[:, k, :],
                                  start=(k == 0), stop=(k == M - 1))
                last.then_inc(signal, 1)

            def ffn(f, g):
                turn(2 * f, g)
                pe.wait_ge(s["mixed"], g * 4 + 2 * f + 1)
                cols_out(2, w["k_ffn"], XK, s["k_psum"])
                pe.wait_ge(s["mixed"], g * 4 + 2 * f + 2)
                rows_out(4, w["r_ffn"], XR, s["r_psum"])
                pe.wait_ge(s["k_squared"], g * 2 + f + 1)
                rows_out(6, w["v_ffn"], KA, s["v_psum"])

            pe.wait_ge(s["weights_in"], 16 * N_IN)
            with pe.Fori(0, GROUPS) as g:
                ffn(0, g)
                turn(1, g)
                pe.wait_ge(s["xT_ready"], g * 3 + 2)
                cols_out(2, w["q"], YT, s["proj_psum"])
                cols_out(4, w["k"], YT, s["proj_psum"])
                cols_out(6, w["v"], YT, s["proj_psum"])
                cols_out(0, w["g"], YT, s["proj_psum"])
                pe.wait_ge(s["conv_in"], g * 3 + 1)
                for j in range(NT):
                    for k in range(M):
                        last = mm(ps[:, 2 * BANK + j * 2 * NH:2 * BANK + (j + 1) * 2 * NH],
                                  YT[:, k * HALF + j * P:k * HALF + (j + 1) * P], w_ab[:, k, :],
                                  start=(k == 0), stop=(k == M - 1))
                last.then_inc(s["ab_psum"], 1)
                pe.wait_ge(s["g_ready"], g + 1)
                pe.wait_ge(s["beta_ready"], g + 1)
                pe.wait_ge(s["conv_in"], g * 3 + 3)
                for kind in range(2):
                    for m in range(M):
                        for j in range(NT):
                            o = (4 + 2 * kind + m) * BANK + j * P
                            src = (DX, R)[kind]
                            last = nc.tensor.transpose(ps[:, o:o + P], src[:, j * H + m * P:j * H + (m + 1) * P], ident)
                    last.then_inc(s["rep_psum"], 1)
                for i in range(2):
                    pe.wait_ge(s["sq_ready"], g * 2 + i + 1)
                    if i == 0:
                        pe.wait_ge(s["gate_ready"], g + 1)
                    src = DX if i == 0 else R
                    for m in range(M):
                        last = mm(bank(2 * i + m), same_head, src[:, m * HALF:(m + 1) * HALF], start=True, stop=True)
                    last.then_inc(s["ss_psum"], 1)
                pe.wait_ge(s["qk_ready"], g * 2 + 2)
                pe.wait_ge(s["rep_ready"], g * 2 + 2)
                pe.wait_ge(s["kspread"], (g + 1) * 16 * HP)
                pe.wait_ge(s["vspread"], (g + 1) * 16 * HP)
                for i in range(PACKS):
                    o = i * 4 * C
                    kqi = KQI[:].rearrange("p a (c k) -> p a c k", c=C)[:, :, :, i]
                    mm(ps[:, o:o + 3 * C], block_of(spread_a, i), kqi, start=True, stop=True)
                    last = mm(ps[:, o + 3 * C:o + 4 * C], block_of(spread_b, i), kqi[:, 2], start=True, stop=True)
                    if i % C == C - 1:
                        last.then_inc(s["gram_psum"], 1)
                pe.wait_ge(s["gram_out"], g * 4 + 4)
                for t in range(C):
                    turn_ = nc.tensor.transpose if t else (lambda o, i, e: mm(o, i, e, start=True, stop=True))
                    last = turn_(ps[0:PACKS, t * P:(t + 1) * P], packs(KA[:])[:, :, t], ident)
                last.then_inc(s["a_psum"], 1)
                pe.wait_ge(s["inv_ready"], g + 1)
                for t in range(C):
                    turn_ = nc.tensor.transpose if t else (lambda o, i, e: mm(o, i, e, start=True, stop=True))
                    last = turn_(ps[:, 4 * BANK + t * PACKS:4 * BANK + (t + 1) * PACKS],
                                               Tu[:, t * P:(t + 1) * P], ident[0:PACKS, 0:PACKS])
                last.then_inc(s["t_psum"], 1)
                pe.wait_ge(s["ttb_ready"], g + 1)
                pe.wait_ge(s["ktspread"], (g + 1) * 16 * HP)
                for i in range(PACKS):
                    last = mm(ps[:, i * C:i * C + C], block_of(spread_b, i), XK[:, i * C:i * C + C],
                              start=True, stop=True)
                last.then_inc(s["uw_psum"], 1)
                pe.wait_ge(s["tspread"], (g + 1) * 16 * HP)
                for i in range(PACKS):
                    o = 6 * BANK + i * C
                    last = mm(ps[:, o:o + C], block_of(spread_a, i), YT[:, i * C:i * C + C],
                              start=True, stop=True)
                last.then_inc(s["uw_psum"], 1)
                pe.wait_ge(s["s0_ready"], g + 1)
                pe.wait_ge(s["wspread"], (g + 1) * 16 * HP)
                for n in range(NCH):
                    for b in range(B):
                        if n:
                            pe.wait_ge(s["s_ready"], g * NCH * B + n * B - B + b + 1)
                        for m in range(M):
                            i = (m * B + b) * NCH + n
                            o = (2 + b) * BANK + (n * M + m) * D
                            last = mm(ps[:, o:o + D], block_of(spread_c, i), turned(KA[:])[:, i, :],
                                      start=True, stop=True)
                        last.then_inc(s["pred_psum"], 1)
                    for b in range(B):
                        pe.wait_ge(s["delta_ready"], g * NCH * B + n * B + b + 1)
                        for m in range(M):
                            i = (m * B + b) * NCH + n
                            o = (4 + b) * BANK + (n * M + m) * D
                            last = mm(ps[:, o:o + D], block_of(spread_b, i), fD[:, b, m, :],
                                      start=True, stop=True)
                        last.then_inc(s["snew_psum"], 1)
                pe.wait_ge(s["uw_ready"], g * 2 + 2)
                pe.wait_ge(s["sspread"], (g + 1) * 16 * HP)
                pe.wait_ge(s["dspread"], (g + 1) * 16 * HP)
                for i in range(PACKS):
                    o = 6 * BANK + i * C
                    mm(ps[:, o:o + C], block_of(spread_a, i), turned(KQI[:, 1, :])[:, i, :], start=True, stop=False)
                    last = mm(ps[:, o:o + C], block_of(spread_b, i), R[:, i * C:i * C + C], start=False, stop=True)
                last.then_inc(s["o_psum"], 1)
                pe.wait_ge(s["osq_ready"], g + 1)
                for m in range(M):
                    last = mm(bank(m), same_head, DX[:, m * HALF:(m + 1) * HALF], start=True, stop=True)
                last.then_inc(s["oss_psum"], 1)
                pe.wait_ge(s["og_ready"], g + 1)
                rows_out(2, w["o"], OT, s["wo_psum"])
                ffn(1, g)

        @block.scalar
        def _(act):
            af = nc.scalar.activation
            own = Steps(act, s["act_step"], ACT_STEPS)

            def std_and_turn(u, g):
                act.wait_ge(s["stats_ready"], g * 3 + u + 1)
                af(sd[:], mv[:, :, 1:2], ACT.Sqrt).then_inc(s["std_ready"], 1)
                act.wait_ge(s["xT_psum"], g * 3 + u + 1)
                if u != 1:
                    f = u // 2
                    for k in range(M):
                        own.done(nc.scalar.copy(XT[:, k, :, 0:1], XTc[:, f, k]))
                        own.done(nc.scalar.copy(XT[:, k, :, 1:], bank(k).rearrange("p (b t) -> p b t", b=B)))
                    own.settle()
                    for k in range(M):
                        last = nc.scalar.copy(XTc[:, f, k], XT[:, k, :, TG:TG + 1])
                        if k < M - 1:
                            own.done(last)
                    last.then_inc(s["xT_ready"], 1)
                else:
                    af(YT[:], bank(0, 2), ACT.Copy).then_inc(s["xT_ready"], 1)

            def ffn(f, g):
                std_and_turn(2 * f, g)
                act.wait_ge(s["k_psum"], g * 2 + f + 1)
                af(KA[:], bank(2, 2), ACT.Relu).then_inc(s["k_relu"], 1)
                act.wait_ge(s["r_psum"], g * 2 + f + 1)
                af(R[:], bank(4, 2), ACT.Sigmoid).then_inc(s["r_ready"], 1)

            act.wait_ge(s["weights_in"], 16 * N_IN)
            af(neg_a[:], a_log, ACT.Exp).then_inc(s["setup_act"], 1)
            act.wait_ge(s["zeroed"], N_ZERO)
            with act.Fori(0, GROUPS) as g:
                own.g, own.k = g, 0
                for b in range(B):
                    act.dma_start(X[:, 2 * b:2 * b + 2, :],
                                  x_v[bass.ds(g, 1), :, b].rearrange("g p q c -> (g p) q c")).then_inc(s["x_in"], 16)
                ffn(0, g)
                std_and_turn(1, g)
                for i in range(3):
                    act.wait_ge(s["proj_psum"], g * 4 + i + 1)
                    for m in range(M):
                        own.done(nc.scalar.copy(CIN[i][:, m, :, 0:CT], cinc[:, i, m]))
                        own.done(nc.scalar.copy(CIN[i][:, m, :, CT:], bank(2 + 2 * i + m).rearrange("p (b t) -> p b t", b=B)))
                    own.settle()
                    for m in range(M):
                        last = nc.scalar.copy(cinc[:, i, m], CIN[i][:, m, :, TG:TG + CT])
                        if m < M - 1:
                            own.done(last)
                    last.then_inc(s["conv_in"], 1)
                act.wait_ge(s["proj_psum"], g * 4 + 4)
                af(GS[:], bank(0, 2), ACT.Silu).then_inc(s["gate_ready"], 1)
                act.wait_ge(s["z_ready"], g + 1)
                beta_in = ps[:, 2 * BANK + NH:2 * BANK + NT * 2 * NH]
                beta_in = bass.AP(tensor=beta_in.tensor, offset=beta_in.offset,
                                  ap=[list(beta_in.ap[0]), [2 * NH, NT], [1, NH], [0, C]])
                af(R[:].rearrange("p (j h c) -> p j h c", h=NH, c=C), beta_in, ACT.Sigmoid).then_inc(s["beta_ready"], 1)
                af(sp[:, 2], sp[:, 1], ACT.Exp, scale=-1.0).then_inc(s["e1_ready"], 1)
                act.wait_ge(s["u_ready"], g + 1)
                af(sp[:, 4], sp[:, 3], ACT.Ln).then_inc(s["ln_ready"], 1)
                for kind, dst in ((0, XR), (1, XK)):
                    act.wait_ge(s["rep_psum"], g * 2 + kind + 1)
                    af(dst[:], bank(4 + 2 * kind, 2), ACT.Copy).then_inc(s["rep_ready"], 1)
                for i, dst, sq in ((0, EE[:], DX), (1, E[:], R), (2, VS[:], None)):
                    act.wait_ge(s["qkv_conv"], g * 3 + i + 1)
                    af(dst, dst, ACT.Silu).then_inc(s["qkv_silu"], 1)
                    if sq is not None:
                        act.wait_ge(s["qkv_silu"], g * 3 + i + 1)
                        af(sq[:], dst, ACT.Square).then_inc(s["sq_ready"], 1)
                for i, dst in ((0, DX), (1, R)):
                    act.wait_ge(s["ss_ready"], g * 2 + i + 1)
                    af(dst[:], dst[:], ACT.Sqrt).then_inc(s["ss_root"], 1)
                act.wait_ge(s["csum_ready"], g + 1)
                af(EE[:], EE[:], ACT.Exp).then_inc(s["ee_ready"], 1)
                act.wait_ge(s["dsum_ready"], g + 1)
                af(E[:], E[:], ACT.Exp).then_inc(s["e_ready"], 1)
                act.wait_ge(s["a_psum"], g + 1)
                af(Au, ps[0:PACKS, 0:C * P], ACT.Copy).then_inc(s["a_ready"], 1)
                act.wait_ge(s["t_psum"], g + 1)
                af(VS[:], bank(4, 2), ACT.Copy).then_inc(s["tt_ready"], 1)
                act.wait_ge(s["uw_psum"], g * 2 + 1)
                af(turned(E[:]), packs(bank(0, 2)), ACT.Copy).then_inc(s["uw_ready"], 1)
                act.wait_ge(s["uw_psum"], g * 2 + 2)
                af(DX[:], bank(6, 2), ACT.Copy).then_inc(s["uw_ready"], 1)
                act.wait_ge(s["o_psum"], g + 1)
                af(DX[:], bank(6, 2), ACT.Square).then_inc(s["osq_ready"], 1)
                act.wait_ge(s["oss_ready"], g + 1)
                af(DX[:], DX[:], ACT.Sqrt).then_inc(s["oss_root"], 1)
                ffn(1, g)
                act.wait_ge(s["x1_ready"], g * 2 + 2)
                for b in range(B):
                    act.dma_start(o_v[bass.ds(g, 1), :, b].rearrange("g p q c -> (g p) q c"),
                                  R[:].rearrange("p (j c) -> p j c", c=H)[:, 2 * b:2 * b + 2, :]).then_inc(s["out_stored"], 16)
                act.wait_ge(s["out_stored"], (g + 1) * B * 16)
                assert own.k == ACT_STEPS, own.k
            act.wait_ge(s["out_stored"], GROUPS * B * 16)

        @block.gpsimd
        def _(pool):
            nc.gpsimd.memset(spread_a[:], 0.0).then_inc(s["zeroed"], 1)
            nc.gpsimd.memset(spread_b[:], 0.0).then_inc(s["zeroed"], 1)
            nc.gpsimd.memset(spread_c[:], 0.0).then_inc(s["zeroed"], 1)
            with pool.Fori(0, GROUPS) as g:
                def square_relu(f):
                    pool.wait_ge(s["k_relu"], g * 2 + f + 1)
                    nc.gpsimd.tensor_tensor(KA[:], KA[:], KA[:], ALU.mult).then_inc(s["k_squared"], 1)
                square_relu(0)
                square_relu(1)

        @block.vector
        def _(ve):
            tt, ts, stt = nc.vector.tensor_tensor, nc.vector.tensor_scalar, nc.vector.scalar_tensor_tensor
            own = Steps(ve, s["vec_step"], VEC_STEPS)

            def chained(ins):
                own.done(ins)
                own.settle()

            def norm(u, g):
                for j in range(NT):
                    own.done(nc.vector.bn_stats(st[:, j, :], X[:, j, :]))
                own.settle()
                nc.vector.memset(fD[:, 0, 0, 0:1], 0.0)
                for j in range(NT):
                    own.done(nc.vector.bn_aggr(mv[:, j, :], st[:, j, :]))
                own.settle()
                ts(mv[:, :, 1:2], mv[:, :, 1:2], 1e-5, None, ALU.add).then_inc(s["stats_ready"], 1)
                ve.wait_ge(s["std_ready"], g * 3 + u + 1)
                chained(nc.vector.reciprocal(rstd[:], sd[:]))
                for j in range(NT):
                    last = ts(XN[:, j * H:(j + 1) * H], X[:, j, :], mv[:, j, 0:1], rstd[:, j, :], ALU.subtract, ALU.mult)
                    if j < NT - 1:
                        own.done(last)
                last.then_inc(s["xn_ready"], 1)

            def ffn(f, g):
                norm(2 * f, g)
                ve.wait_ge(s["xT_ready"], g * 3 + 2 * f + 1)
                now = XT[:, :, :, 1:].rearrange("p m b t -> p (m b) t")
                before = XT[:, :, :, 0:TG].rearrange("p m b t -> p (m b) t")
                chained(tt(packed4(DX), now, before, ALU.subtract))
                for kind, dst in ((1, XK), (0, XR)):
                    for m in range(M):
                        last = stt(packed4(dst)[:, m * B:(m + 1) * B], packed4(DX)[:, m * B:(m + 1) * B],
                                   mu[:, kind, m:m + 1], before[:, m * B:(m + 1) * B], ALU.mult, ALU.add)
                        if m < M - 1:
                            own.done(last)
                    last.then_inc(s["mixed"], 1)
                ve.wait_ge(s["v_psum"], g * 2 + f + 1)
                ve.wait_ge(s["r_ready"], g * 2 + f + 1)
                chained(stt(R[:], bank(6, 2), 0.5, R[:], ALU.mult, ALU.mult))
                Xf = X[:].rearrange("p j c -> p (j c)")
                if f == 0:
                    tt(Xf, Xf, R[:], ALU.add).then_inc(s["x1_ready"], 1)
                    ve.wait_ge(s["x1_ready"], g * 2 + 1)
                else:
                    tt(R[:], Xf, R[:], ALU.add).then_inc(s["x1_ready"], 1)

            def packed4(t):
                return t[:].rearrange("p (a t) -> p a t", t=TG)

            for t in (XTc[:].rearrange("p a b c d -> p (a b c d)"), cinc[:].rearrange("p a b c d -> p (a b c d)"),
                      S_in[:].rearrange("p a b -> p (a b)")):
                nc.vector.memset(t, 0.0).then_inc(s["zeroed"], 1)
            ve.wait_ge(s["setup_act"], 1)
            ts(neg_a[:], neg_a[:], -1.0, None, ALU.mult).then_inc(s["setup_vec"], 1)
            ve.wait_ge(s["setup_vec"], 1)
            ve.wait_ge(s["zeroed"], N_ZERO)
            ve.wait_ge(s["weights_in"], 16 * N_IN)

            with ve.Fori(0, GROUPS) as g:
                own.g, own.k = g, 0
                ve.wait_ge(s["x_in"], (g + 1) * B * 16)
                ffn(0, g)
                norm(1, g)
                ve.wait_ge(s["ab_psum"], g + 1)
                ab = ps[:, 2 * BANK:2 * BANK + NT * 2 * NH].rearrange("p (j k) -> p j k", j=NT)
                chained(tt(sp[:, 0].rearrange("p (j h) -> p j h", h=NH), ab[:, :, 0:NH],
                           dt_b.rearrange("p (j h) -> p j h", h=NH), ALU.add))
                stt(sp[:, 1], sp[:, 0], -1.0, sp[:, 0], ALU.mult, ALU.max).then_inc(s["z_ready"], 1)
                ve.wait_ge(s["e1_ready"], g + 1)
                ts(sp[:, 3], sp[:, 2], 1.0, None, ALU.add).then_inc(s["u_ready"], 1)
                ve.wait_ge(s["u_ready"], g + 1)
                own.done(nc.vector.reciprocal(sp[:, 6], sp[:, 3]))
                chained(ts(sp[:, 5], sp[:, 3], -1.0, None, ALU.add))
                chained(tt(sp[:, 5], sp[:, 2], sp[:, 5], ALU.subtract))
                chained(tt(sp[:, 5], sp[:, 5], sp[:, 6], ALU.mult))
                ve.wait_ge(s["ln_ready"], g + 1)
                chained(tt(sp[:, 4], sp[:, 4], sp[:, 5], ALU.add))
                chained(stt(sp[:, 5], sp[:, 0], 0.0, sp[:, 4], ALU.max, ALU.add))
                tt(packs(DX[:]), rep(sp[:, 5], C), rep(neg_a[:], C), ALU.mult).then_inc(s["g_ready"], 1)
                for i, src, dst in ((0, 1, EE[:]), (1, 0, E[:]), (2, 2, VS[:])):
                    ve.wait_ge(s["conv_in"], g * 3 + src + 1)
                    d4 = dst.rearrange("p (m b t) -> p m b t", m=M, b=B)
                    for tap in range(KC):
                        for m in range(M):
                            if tap == 0:
                                last = ts(d4[:, m], CIN[src][:, m, :, 0:TG], cw[:, src, m, 0:1], None, ALU.mult)
                            else:
                                last = stt(d4[:, m], CIN[src][:, m, :, tap:tap + TG], cw[:, src, m, tap:tap + 1],
                                           d4[:, m], ALU.mult, ALU.add)
                            if tap < KC - 1 or m < M - 1:
                                own.done(last)
                        if tap < KC - 1:
                            own.settle()
                    last.then_inc(s["qkv_conv"], 1)
                for i, buf, f2 in ((0, DX, 1.0), (1, R, float(D))):
                    ve.wait_ge(s["ss_psum"], g * 2 + i + 1)
                    ts(buf[:], bank(2 * i, 2), 1e-6, f2, ALU.add, ALU.mult).then_inc(s["ss_ready"], 1)
                for i, buf, val in ((0, DX, EE), (1, R, E)):
                    ve.wait_ge(s["ss_root"], g * 2 + i + 1)
                    chained(nc.vector.reciprocal(buf[:], buf[:]))
                    tt(turned(KQI[:, i, :]), packs(val[:]), packs(buf[:]), ALU.mult).then_inc(s["qk_ready"], 1)
                ve.wait_ge(s["rep_ready"], g * 2 + 2)
                ve.wait_ge(s["qkv_silu"], g * 3 + 3)
                tt(turned(YT[:]), packs(VS[:]), packs(XK[:]), ALU.mult).then_inc(s["vb_ready"], 1)
                nc.vector.tensor_tensor_scan(EE[:], notfirst[:], XR[:], 0.0, ALU.mult, ALU.add).then_inc(s["csum_ready"], 1)
                chained(tt(packs(DX[:]), packs(XR[:]), bc(msk[:, 0, :], PACKS), ALU.mult))
                nc.vector.tensor_tensor_scan(E[:], notfirst[:], DX[:], 0.0, ALU.mult, ALU.add).then_inc(s["dsum_ready"], 1)
                ve.wait_ge(s["ee_ready"], g + 1)
                ve.wait_ge(s["dsum_ready"], g + 1)
                chained(tt(DX[:], XK[:], EE[:], ALU.mult))
                chained(tt(packs(DX[:]), packs(DX[:]), bc(msk[:, 2, :], PACKS), ALU.mult))
                own.done(nc.vector.tensor_reduce(be[:], packs(DX[:]), AX_X, ALU.add))
                ve.wait_ge(s["e_ready"], g + 1)
                own.done(nc.vector.tensor_copy(fd[:], packs(E[:])[:, :, C - 1]))
                own.done(tt(packs(R[:]), packs(E[:]), bc(msk[:, 1, :], PACKS), ALU.mult))
                chained(tt(KA[:], XK[:], E[:], ALU.mult))
                chained(tt(packs(KA[:]), packs(KA[:]), bc(msk[:, 0, :], PACKS), ALU.mult))
                for r in range(4):
                    ve.wait_ge(s["gram_psum"], g * 4 + r + 1)
                    src = ps[:, r * 2 * BANK:(r + 1) * 2 * BANK].rearrange("p (k c) -> p k c", c=4 * C)
                    sl = slice(r * C * C, (r + 1) * C * C)
                    own.done(stt(packs(KA[:, sl]), src[:, :, 0:C], -1.0, packs(KA[:, sl]), ALU.mult, ALU.mult))
                    own.done(tt(packs(R[:, sl]), src[:, :, C:2 * C], packs(R[:, sl]), ALU.mult))
                    own.done(nc.vector.tensor_copy(turned(XN[:])[:, r * C:(r + 1) * C, :], src[:, :, 2 * C:3 * C]))
                    nc.vector.tensor_copy(packs(YT[:, sl]), src[:, :, 3 * C:4 * C]).then_inc(s["gram_out"], 1)
                own.done(tt(turned(KQI[:, 1, :]), turned(KQI[:, 1, :]), packs(EE[:]), ALU.mult))
                T4 = Tu.rearrange("p (t h c) -> p h t c", t=C, h=HP)
                A4 = Au.rearrange("p (t h c) -> p h t c", t=C, h=HP)
                ve.wait_ge(s["gram_out"], g * 4 + 4)
                ve.wait_ge(s["qkv_conv"], g * 3 + 3)
                own.done(nc.vector.memset(Tu, 0.0))
                own.settle()
                for t in range(C):
                    own.done(nc.vector.memset(T4[:, :, t, t:t + 1], 1.0))
                own.settle()
                ve.wait_ge(s["a_ready"], g + 1)
                for j in range(C - 1):
                    ni, ncol = C - 1 - j, j + 1
                    for h0 in range(0, HP, HP):
                        a_j = A4[:, :, j + 1:C, j]
                        t_j = T4[:, :, j, 0:ncol]
                        a_b = bass.AP(tensor=a_j.tensor, offset=a_j.offset, ap=[list(v) for v in a_j.ap] + [[0, ncol]])
                        t_b = bass.AP(tensor=t_j.tensor, offset=t_j.offset,
                                      ap=[list(t_j.ap[0]), list(t_j.ap[1]), [0, ni]] + [list(v) for v in t_j.ap[2:]])
                        if len(t_j.ap) == 2:
                            t_b = bass.AP(tensor=t_j.tensor, offset=t_j.offset, ap=[list(t_j.ap[0]), list(t_j.ap[1]), [0, ni], [1, 1]])
                        pr = prod[:, 0:HP * ni * ncol].rearrange("p (h i c) -> p h i c", h=HP, i=ni)
                        chained(tt(pr, a_b, t_b, ALU.mult))
                        t_i = T4[:, :, j + 1:C, 0:ncol]
                        last = tt(t_i, t_i, pr, ALU.add)
                        if j < C - 2:
                            chained(last)
                last.then_inc(s["inv_ready"], 1)
                ve.wait_ge(s["tt_ready"], g + 1)
                tt(packs(XK[:]), turned(VS[:]), rep(be[:], C), ALU.mult).then_inc(s["ttb_ready"], 1)
                states = KA[:].rearrange("p (d mb n) -> p mb n d", n=NCH, d=D)
                deltas = XR[:].rearrange("p (d m b n) -> p b n m d", m=M, b=B, n=NCH)
                us = DX[:].rearrange("p (m b n d) -> p b n m d", m=M, b=B, n=NCH)
                fds = fd[:].rearrange("p (m b n) -> p b n m", m=M, b=B)
                ve.wait_ge(s["a_psum"], g + 1)
                nc.vector.tensor_copy(states[:, :, 0, :], S_in[:]).then_inc(s["s0_ready"], 1)
                ve.wait_ge(s["s0_ready"], g + 1)
                ve.wait_ge(s["uw_ready"], g * 2 + 2)
                for n in range(NCH):
                    for b in range(B):
                        ve.wait_ge(s["pred_psum"], g * NCH * B + n * B + b + 1)
                        o = (2 + b) * BANK + n * M * D
                        chained(tt(deltas[:, b, n], us[:, b, n], ps[:, o:o + M * D].rearrange("p (m d) -> p m d", m=M), ALU.subtract))
                        f_n = fds[:, b, n]
                        tt(fD[:, b], deltas[:, b, n], bass.AP(tensor=f_n.tensor, offset=f_n.offset,
                           ap=[list(f_n.ap[0]), list(f_n.ap[1]), [0, D]]), ALU.mult).then_inc(s["delta_ready"], 1)
                    for b in range(B):
                        ve.wait_ge(s["snew_psum"], g * NCH * B + n * B + b + 1)
                        for m in range(M):
                            i = (m * B + b) * NCH + n
                            dst = states[:, m * B + b, n + 1, :] if n < NCH - 1 else S_in[:, m * B + b, :]
                            o = (4 + b) * BANK + (n * M + m) * D
                            last = stt(dst, states[:, m * B + b, n, :], EE[:, i * C + C - 1:i * C + C], ps[:, o:o + D],
                                       ALU.mult, ALU.add)
                            if m < M - 1:
                                own.done(last)
                        last.then_inc(s["s_ready"], 1)
                    if n < NCH - 1:
                        ve.wait_ge(s["s_ready"], g * NCH * B + (n + 1) * B)
                ve.wait_ge(s["oss_psum"], g + 1)
                ts(DX[:], bank(0, 2), 1.0 / D, 1e-5, ALU.mult, ALU.add).then_inc(s["oss_ready"], 1)
                ve.wait_ge(s["oss_root"], g + 1)
                chained(nc.vector.reciprocal(DX[:], DX[:]))
                chained(stt(OT, bank(6, 2), normw, DX[:], ALU.mult, ALU.mult))
                tt(OT, OT, GS[:], ALU.mult).then_inc(s["og_ready"], 1)
                ve.wait_ge(s["wo_psum"], g + 1)
                Xf = X[:].rearrange("p j c -> p (j c)")
                chained(tt(Xf, Xf, bank(2, 2), ALU.add))
                ffn(1, g)
                assert own.k == VEC_STEPS, own.k


VEC_N, ACT_N = 208, 25
N_IN, N_ZERO = 16, 6

WEIGHTS = {"r_ffn": "L0_ffn_W_r", "k_ffn": "L0_ffn_W_k", "v_ffn": "L0_ffn_W_v", "q": "L0_attn_Wq", "k": "L0_attn_Wk",
           "v": "L0_attn_Wv", "g": "L0_attn_Wg", "o": "L0_attn_Wo"}


def kernel(**inputs):
    import concourse.bacc as _bacc
    from concourse.bass_utils import run_bass_kernel_spmd as _run

    a = {n: np.asarray(v) for n, v in inputs.items()}
    p, c = np.arange(P)[:, None], np.arange(C)[None, :]
    cols = np.arange(COLS)[None, :]
    halves = lambda v: np.stack([v[:P], v[P:]], 1)
    arrays = {"x": np.ascontiguousarray(a["L0_attn_hidden"])}
    for n, full in WEIGHTS.items():
        arrays[f"wT_{n}"] = np.ascontiguousarray(a[full].T)
    arrays["wT_ab"] = np.ascontiguousarray(np.concatenate([a["L0_attn_Wa"], a["L0_attn_Wb"]]).T)
    arrays["mu"] = np.ascontiguousarray(np.stack([halves(a["L0_ffn_mu_r"]), halves(a["L0_ffn_mu_k"])], 1))
    arrays["convw"] = np.ascontiguousarray(np.stack([halves(a[f"L0_attn_conv_{n}"]) for n in "qkv"], 1))
    arrays["headp"] = np.ascontiguousarray(np.concatenate([
        np.tile(a["L0_attn_norm_w"], HP)[:, None], np.tile(a["L0_attn_A_log"], (P, NT)),
        np.tile(a["L0_attn_dt_bias"], (P, NT))], 1))
    arrays["consts"] = np.ascontiguousarray(np.concatenate([
        np.eye(P), p // C == np.arange(P)[None, :] // C, c > p % C, c >= p % C, c == p % C,
        np.broadcast_to(cols % C != 0, (P, COLS)), cols // PACKS == p % C], 1).astype(np.float32))

    nc = _bacc.Bacc("TRN2", target_bir_lowering=False, num_devices=1)
    ap = {n: nc.dram_tensor(f"in_{n}", v.shape, mybir.dt.from_np(v.dtype), kind="ExternalInput").ap()
          for n, v in arrays.items()}
    out = nc.dram_tensor("out_x", (B, SEQ, H), F32, kind="ExternalOutput").ap()
    macaron_kernel(nc, ap["x"], {n: ap[f"wT_{n}"] for n in WEIGHTS}, ap["mu"], ap["convw"], ap["wT_ab"],
                   ap["headp"], ap["consts"], out)
    r = _run(nc, [{f"in_{n}": v for n, v in arrays.items()}], core_ids=[0])
    return r.results[0]["out_x"]
```
